# Optimizing a Trainium2 kernel written in Bass

```python
import numpy as np
import jax
import jax.numpy as jnp

def _softmax(x, axis=-1):
    return jax.nn.softmax(x, axis=axis)

def _gelu(x):
    return jax.nn.gelu(x, approximate=True)

def _silu(x):
    return jax.nn.silu(x)

def _sigmoid(x):
    return jax.nn.sigmoid(x)

def _layernorm(x, axis=-1, eps=1e-05):
    m = jnp.mean(x, axis=axis, keepdims=True)
    v = jnp.var(x, axis=axis, keepdims=True)
    return (x - m) / jnp.sqrt(v + eps)

def _scatter_add(tgt, idx, src, axis=0):
    return tgt.at[idx].add(src)

def _segment_sum(src, seg, n):
    return jax.ops.segment_sum(src, seg, n)
kernel_name = 'mk_rec_standalone_d1_rec_r8_252215'

def setup_inputs(seed: int=0):
    np.random.seed(seed)
    _w = jnp.asarray

    def _rec_inputs():
        import jax
        import jax.numpy as jnp
        _rk = jax.random.key(seed)
        r_x = -0.000123307 + 1.00004 * jax.random.normal(jax.random.fold_in(_rk, 1), (512, 40, 128), jnp.float32)
        return r_x
    r_x = _rec_inputs()

    def _L0_rec_setup():
        import jax, jax.numpy as jnp
        import numpy as np
        NUM_FEAT = 40
        EMBED_DIM = 128
        BATCH = 256
        _I, _J = np.triu_indices(NUM_FEAT, k=1)
        PAIR_I = jnp.asarray(_I, dtype=jnp.int32)
        PAIR_J = jnp.asarray(_J, dtype=jnp.int32)
        key = jax.random.key(seed)
        k1, k2 = jax.random.split(key)
        x = jax.random.normal(k1, (BATCH, NUM_FEAT, EMBED_DIM), dtype=jnp.float32)
        W = jax.random.normal(k2, (EMBED_DIM, EMBED_DIM), dtype=jnp.float32) * (1.0 / np.sqrt(EMBED_DIM))
        return {'x': x, 'W': W}
    _L0_rec_all = _L0_rec_setup()
    _L0_rec_in = {k: v for k, v in _L0_rec_all.items() if k in ('W',)}
    del _L0_rec_all
    return {'r_x': r_x, 'L0_rec_W': _L0_rec_in['W']}

def reference(r_x, L0_rec_W):
    import jax
    import jax.numpy as jnp

    def _L0_rec_ref(x, W):
        import jax, jax.numpy as jnp
        import numpy as np
        NUM_FEAT = 40
        EMBED_DIM = 128
        BATCH = 256
        _I, _J = np.triu_indices(NUM_FEAT, k=1)
        PAIR_I = jnp.asarray(_I, dtype=jnp.int32)
        PAIR_J = jnp.asarray(_J, dtype=jnp.int32)
        proj = jnp.einsum('bnd,ed->bne', x, W)
        out = proj[:, PAIR_I, :] * proj[:, PAIR_J, :]
        return out
    y = _L0_rec_ref(r_x, L0_rec_W)
    return y

_drawn_inputs = setup_inputs


def setup_inputs(seed=0):
    import zlib

    import numpy as np

    out = dict(_drawn_inputs(seed))
    spreads = {}
    factors = {}
    for name, (base, spread) in spreads.items():
        noise = np.random.default_rng([zlib.crc32(name.encode()), seed]).standard_normal(out[name].shape)
        drawn = base * np.exp(spread * noise) if base else spread * noise
        out[name] = jnp.asarray(drawn.astype(out[name].dtype))
    for name, factor in factors.items():
        out[name] = (out[name] * factor).astype(out[name].dtype)
    return out
```

```python
import numpy as np
import concourse.bass as bass
from concourse import mybir
from contextlib import ExitStack

P = 128
FEATURES = 40
DIM = 128
PAIRS = FEATURES * (FEATURES - 1) // 2
FIRST_PAIR = [i * (FEATURES - 1) - i * (i - 1) // 2 for i in range(FEATURES)]

LOAD_FEATURES = 4
LOADS = FEATURES // LOAD_FEATURES
GROUP = 2
BANK_FEATURES = 2048 // (4 * DIM)
GROUPS = FEATURES // GROUP
GROUPS_PER_LOAD = LOAD_FEATURES // GROUP

CHUNK = 20
CHUNKS = PAIRS // CHUNK
SLOTS = 13
ROUNDS = CHUNKS // SLOTS

assert LOADS * LOAD_FEATURES == FEATURES and GROUPS * GROUP == FEATURES
assert CHUNKS * CHUNK == PAIRS and ROUNDS * SLOTS == CHUNKS and GROUPS % 2 == 0
assert GROUP <= BANK_FEATURES and LOAD_FEATURES % GROUP == 0


def load_range(load):
    return FEATURES - (load + 1) * LOAD_FEATURES, FEATURES - load * LOAD_FEATURES


def group_range(group):
    return FEATURES - (group + 1) * GROUP, FEATURES - group * GROUP


def chunk_range(chunk):
    return PAIRS - (chunk + 1) * CHUNK, PAIRS - chunk * CHUNK


def chunk_rows(chunk):
    low, high = chunk_range(chunk)
    rows = []
    for i in reversed(range(FEATURES - 1)):
        a, b = max(low, FIRST_PAIR[i]), min(high, FIRST_PAIR[i + 1])
        if a < b:
            rows.append((i, i + 1 + a - FIRST_PAIR[i], b - a, a - low))
    return rows


def group_of(i):
    return (FEATURES - 1 - i) // GROUP


def groups_for(chunk):
    return group_of(chunk_rows(chunk)[-1][0]) + 1 if chunk >= 0 else 0


def pairwise_products(nc, x, w, out):
    fp32 = mybir.dt.float32
    ALU = mybir.AluOpType
    tiles = x.shape[0] // P
    assert x.shape[0] == tiles * P

    with ExitStack() as ctx:
        def sbuf(name, shape):
            return ctx.enter_context(nc.sbuf_tensor(name, shape, fp32))

        def psum(name, shape):
            return ctx.enter_context(nc.psum_tensor(name, shape, fp32))

        def sem(name):
            return ctx.enter_context(nc.semaphore(name))

        x_in = sbuf("x_in", [P, FEATURES, DIM])
        proj = sbuf("proj", [P, 2, FEATURES, DIM])
        products = [sbuf(f"products{s}", [P, CHUNK, DIM]) for s in range(SLOTS)]
        x_turned = [sbuf(f"x_turned{k}", [DIM, GROUP, P]) for k in range(2)]
        w_in = sbuf("w_in", [DIM, DIM])
        w_turned = sbuf("w_turned", [DIM, DIM])
        identity = sbuf("identity", [P, P])

        turned_ps = [psum(f"turned_ps{k}", [DIM, BANK_FEATURES, P]) for k in range(2)]
        proj_ps = [psum(f"proj_ps{k}", [P, BANK_FEATURES, DIM]) for k in range(2)]
        w_ps = psum("w_ps", [DIM, DIM])

        w_loaded = sem("w_loaded")
        x_loaded = [sem(f"x_loaded{k}") for k in range(LOADS)]
        identity_zeroed = sem("identity_zeroed")
        identity_made = sem("identity_made")
        w_in_ps = sem("w_in_ps")
        w_ready = sem("w_ready")
        group_turned = sem("group_turned")
        x_turned_ready = sem("x_turned_ready")
        group_projected = sem("group_projected")
        proj_ready = sem("proj_ready")
        chunk_ready = sem("chunk_ready")
        proj_free = sem("proj_free")
        stored = [sem(f"stored{s}") for s in range(SLOTS)]

        block = ctx.enter_context(nc.Block())

        @block.sync
        def _(sp):
            for load in range(LOADS):
                a, b = load_range(load)
                sp.dma_start(x_in[:, a:b, :], x[0:P, a:b, :]).then_inc(x_loaded[load], 16)
            with sp.Fori(0, tiles) as tile:
                for chunk in range(CHUNKS):
                    a, b = chunk_range(chunk)
                    sp.wait_ge(chunk_ready, tile * CHUNKS + (chunk + 1))
                    sp.nop(nofuse=True)
                    sp.dma_start(out[bass.ds(tile * P, P), a:b, :],
                                 products[chunk % SLOTS][:, :, :]).then_inc(stored[chunk % SLOTS], 16)
            for slot in range(SLOTS):
                sp.wait_ge(stored[slot], 16 * tiles * ROUNDS)

        @block.gpsimd
        def _(pool):
            pool.memset(identity[:, :], 0.0).then_inc(identity_zeroed, 1)
            pool.wait_ge(identity_zeroed, 1)
            pool.affine_select(out=identity[:, :], in_=identity[:, :], compare_op=ALU.not_equal, fill=1.0,
                               base=0, pattern=[[-1, P]], channel_multiplier=1).then_inc(identity_made, 1)

        @block.tensor
        def _(pe):
            pe.wait_ge(identity_made, 1)
            pe.wait_ge(w_loaded, 16)
            pe.transpose(w_ps[:, :], w_in[:, :], identity[:, :]).then_inc(w_in_ps, 1)
            pe.wait_ge(w_ready, 1)

            with pe.Fori(0, tiles) as tile:
                def turn(group):
                    if group % GROUPS_PER_LOAD == 0:
                        pe.wait_ge(x_loaded[group // GROUPS_PER_LOAD], 16 * tile + 16)
                    a, b = group_range(group)
                    for n in range(a, b):
                        last = pe.transpose(turned_ps[group % 2][:, n - a, :], x_in[:, n, :], identity[:, :])
                    last.then_inc(group_turned, 1)

                def project(group):
                    pe.wait_ge(x_turned_ready, tile * GROUPS + (group + 1))
                    if group >= 2:
                        pe.wait_ge(proj_ready, tile * GROUPS + (group - 1))
                    for k in range(GROUP):
                        last = pe.matmul(proj_ps[group % 2][:, k, :], x_turned[group % 2][:, k, :], w_turned[:, :],
                                         start=True, stop=True)
                    last.then_inc(group_projected, 1)

                turn(0)
                for group in range(1, GROUPS):
                    turn(group)
                    project(group - 1)
                project(GROUPS - 1)
                pe.wait_ge(proj_ready, tile * GROUPS + GROUPS)

        @block.scalar
        def _(act):
            act.dma_start(w_in[:, :], w).then_inc(w_loaded, 16)
            act.wait_ge(w_in_ps, 1)
            act.copy(w_turned[:, :], w_ps[:, :]).then_inc(w_ready, 1)

            def carry_turned(tile, group):
                act.wait_ge(group_turned, tile * GROUPS + (group + 1))
                act.copy(x_turned[group % 2][:, :, :], turned_ps[group % 2][:, 0:GROUP, :]).then_inc(x_turned_ready, 1)

            def load_next(tile, load):
                a, b = load_range(load)
                act.dma_start(x_in[:, a:b, :], x[bass.ds((tile + 1) * P, P), a:b, :]).then_inc(x_loaded[load], 16)

            def carry_projected(tile, group):
                a, b = group_range(group)
                act.wait_ge(group_projected, tile * GROUPS + (group + 1))
                act.copy(proj[:, tile % 2, a:b, :], proj_ps[group % 2][:, 0:GROUP, :]).then_inc(proj_ready, 1)

            with act.Fori(0, tiles - 1) as tile:
                act.wait_ge(proj_free, tile + 1)
                carry_turned(tile, 0)
                for group in range(1, GROUPS):
                    carry_turned(tile, group)
                    if group % GROUPS_PER_LOAD == GROUPS_PER_LOAD - 1:
                        load_next(tile, group // GROUPS_PER_LOAD)
                    carry_projected(tile, group - 1)
                carry_projected(tile, GROUPS - 1)
            act.wait_ge(proj_free, tiles)
            carry_turned(tiles - 1, 0)
            for group in range(1, GROUPS):
                carry_turned(tiles - 1, group)
                carry_projected(tiles - 1, group - 1)
            carry_projected(tiles - 1, GROUPS - 1)

        @block.vector
        def _(dve):
            def multiply_chunk(tile, chunk):
                slot = chunk % SLOTS
                first_group = groups_for(chunk - 1)
                for i, j, count, place in chunk_rows(chunk):
                    group = group_of(i)
                    if group >= first_group:
                        first_group = group + 1
                        dve.wait_ge(proj_ready, tile * GROUPS + (group + 1))
                    last = dve.tensor_tensor(
                        products[slot][:, place:place + count, :],
                        proj[:, tile % 2, i:i + 1, :].broadcast_to([P, count, DIM]),
                        proj[:, tile % 2, j:j + count, :], ALU.mult)
                last.then_inc(chunk_ready, 1)

            def give_back(tile):
                dve.wait_ge(chunk_ready, tile * CHUNKS + CHUNKS)
                dve.sem_inc(proj_free, 1)

            dve.sem_inc(proj_free, 2)
            for chunk in range(CHUNKS):
                if chunk >= SLOTS:
                    dve.wait_ge(stored[chunk % SLOTS], 16 * (chunk // SLOTS))
                multiply_chunk(0, chunk)
            give_back(0)
            with dve.Fori(1, tiles) as tile:
                for chunk in range(CHUNKS):
                    dve.wait_ge(stored[chunk % SLOTS], 16 * ROUNDS * tile + 16 * (chunk // SLOTS))
                    multiply_chunk(tile, chunk)
                give_back(tile)


_INS = ["r_x", "L0_rec_W"]


def kernel(**inputs):
    import concourse.bacc as _bacc
    from concourse.bass_utils import run_bass_kernel_spmd as _run

    nc = _bacc.Bacc("TRN2", target_bir_lowering=False, num_devices=1)
    arrays, args = {}, []
    for name in _INS:
        a = np.ascontiguousarray(inputs[name])
        arrays[f"in_{name}_dram"] = a
        args.append(nc.dram_tensor(f"in_{name}_dram", a.shape, mybir.dt.from_np(a.dtype), kind="ExternalInput").ap())
    shape = (inputs["r_x"].shape[0], PAIRS, DIM)
    args.append(nc.dram_tensor("out_dram", shape, mybir.dt.float32, kind="ExternalOutput").ap())
    pairwise_products(nc, *args)
    r = _run(nc, [arrays], core_ids=[0])
    return r.results[0]["out_dram"]
```

```python
import numpy as np
import concourse.bass as bass
from concourse import mybir
from contextlib import ExitStack

P = 128
FEATURES = 40
DIM = 128
PAIRS = FEATURES * (FEATURES - 1) // 2
FIRST_PAIR = [i * (FEATURES - 1) - i * (i - 1) // 2 for i in range(FEATURES)]

LOAD_FEATURES = 4
LOADS = FEATURES // LOAD_FEATURES
GROUP = 2
BANK_FEATURES = 2048 // (4 * DIM)
GROUPS = FEATURES // GROUP
GROUPS_PER_LOAD = LOAD_FEATURES // GROUP

CHUNK = 39
CHUNKS = PAIRS // CHUNK
SLOTS = 5
ROUNDS = CHUNKS // SLOTS

assert LOADS * LOAD_FEATURES == FEATURES and GROUPS * GROUP == FEATURES
assert CHUNKS * CHUNK == PAIRS and ROUNDS * SLOTS == CHUNKS and GROUPS % 2 == 0
assert GROUP <= BANK_FEATURES and LOAD_FEATURES % GROUP == 0


def load_range(load):
    return FEATURES - (load + 1) * LOAD_FEATURES, FEATURES - load * LOAD_FEATURES


def group_range(group):
    return FEATURES - (group + 1) * GROUP, FEATURES - group * GROUP


def chunk_range(chunk):
    return PAIRS - (chunk + 1) * CHUNK, PAIRS - chunk * CHUNK


def chunk_rows(chunk):
    low, high = chunk_range(chunk)
    rows = []
    for i in reversed(range(FEATURES - 1)):
        a, b = max(low, FIRST_PAIR[i]), min(high, FIRST_PAIR[i + 1])
        if a < b:
            rows.append((i, i + 1 + a - FIRST_PAIR[i], b - a, a - low))
    return rows


def group_of(i):
    return (FEATURES - 1 - i) // GROUP


def groups_for(chunk):
    return group_of(chunk_rows(chunk)[-1][0]) + 1 if chunk >= 0 else 0


def pairwise_products(nc, x, w, out):
    fp32 = mybir.dt.float32
    ALU = mybir.AluOpType
    tiles = x.shape[0] // P
    assert x.shape[0] == tiles * P and tiles % 2 == 0 and tiles >= 4

    with ExitStack() as ctx:
        def sbuf(name, shape):
            return ctx.enter_context(nc.sbuf_tensor(name, shape, fp32))

        def psum(name, shape):
            return ctx.enter_context(nc.psum_tensor(name, shape, fp32))

        def sem(name):
            return ctx.enter_context(nc.semaphore(name))

        x_in = [sbuf(f"x_in{h}", [P, FEATURES, DIM]) for h in range(2)]
        proj = sbuf("proj", [P, 2, FEATURES, DIM])
        products = [sbuf(f"products{s}", [P, CHUNK, DIM]) for s in range(SLOTS)]
        x_turned = [sbuf(f"x_turned{k}", [DIM, GROUP, P]) for k in range(2)]
        w_in = sbuf("w_in", [DIM, DIM])
        w_turned = sbuf("w_turned", [DIM, DIM])
        identity = sbuf("identity", [P, P])

        turned_ps = [psum(f"turned_ps{k}", [DIM, BANK_FEATURES, P]) for k in range(2)]
        proj_ps = [psum(f"proj_ps{k}", [P, BANK_FEATURES, DIM]) for k in range(2)]
        w_ps = psum("w_ps", [DIM, DIM])

        w_loaded = sem("w_loaded")
        x_loaded = [[sem(f"x_loaded{half}_{k}") for k in range(LOADS)] for half in range(2)]
        identity_zeroed = sem("identity_zeroed")
        identity_made = sem("identity_made")
        w_in_ps = sem("w_in_ps")
        w_ready = sem("w_ready")
        group_turned = sem("group_turned")
        x_turned_ready = sem("x_turned_ready")
        group_projected = sem("group_projected")
        proj_ready = sem("proj_ready")
        chunk_ready = sem("chunk_ready")
        proj_free = sem("proj_free")
        stored = [sem(f"stored{s}") for s in range(SLOTS)]

        block = ctx.enter_context(nc.Block())

        @block.sync
        def _(sp):
            for half in range(2):
                for load in range(LOADS):
                    a, b = load_range(load)
                    sp.dma_start(x_in[half][:, a:b, :],
                                 x[half * P:(half + 1) * P, a:b, :]).then_inc(x_loaded[half][load], 16)
            with sp.Fori(0, tiles) as tile:
                for chunk in range(CHUNKS):
                    a, b = chunk_range(chunk)
                    sp.wait_ge(chunk_ready, tile * CHUNKS + (chunk + 1))
                    sp.nop(nofuse=True)
                    sp.dma_start(out[bass.ds(tile * P, P), a:b, :],
                                 products[chunk % SLOTS][:, :, :]).then_inc(stored[chunk % SLOTS], 16)
            for slot in range(SLOTS):
                sp.wait_ge(stored[slot], 16 * tiles * ROUNDS)

        @block.gpsimd
        def _(pool):
            pool.memset(identity[:, :], 0.0).then_inc(identity_zeroed, 1)
            pool.wait_ge(identity_zeroed, 1)
            pool.affine_select(out=identity[:, :], in_=identity[:, :], compare_op=ALU.not_equal, fill=1.0,
                               base=0, pattern=[[-1, P]], channel_multiplier=1).then_inc(identity_made, 1)

        @block.tensor
        def _(pe):
            pe.wait_ge(identity_made, 1)
            pe.wait_ge(w_loaded, 16)
            pe.transpose(w_ps[:, :], w_in[:, :], identity[:, :]).then_inc(w_in_ps, 1)
            pe.wait_ge(w_ready, 1)

            def turn(pair, half, group):
                if group % GROUPS_PER_LOAD == 0:
                    pe.wait_ge(x_loaded[half][group // GROUPS_PER_LOAD], 16 * pair + 16)
                a, b = group_range(group)
                for n in range(a, b):
                    last = pe.transpose(turned_ps[group % 2][:, n - a, :], x_in[half][:, n, :], identity[:, :])
                last.then_inc(group_turned, 1)

            def project(pair, half, group):
                before = pair * 2 * GROUPS + half * GROUPS
                pe.wait_ge(x_turned_ready, before + (group + 1))
                if group >= 2:
                    pe.wait_ge(proj_ready, before + (group - 1))
                for k in range(GROUP):
                    last = pe.matmul(proj_ps[group % 2][:, k, :], x_turned[group % 2][:, k, :], w_turned[:, :],
                                     start=True, stop=True)
                last.then_inc(group_projected, 1)

            with pe.Fori(0, tiles // 2) as pair:
                for half in range(2):
                    turn(pair, half, 0)
                    for group in range(1, GROUPS):
                        turn(pair, half, group)
                        project(pair, half, group - 1)
                    project(pair, half, GROUPS - 1)
                    pe.wait_ge(proj_ready, pair * 2 * GROUPS + (half + 1) * GROUPS)

        @block.scalar
        def _(act):
            act.dma_start(w_in[:, :], w).then_inc(w_loaded, 16)
            act.wait_ge(w_in_ps, 1)
            act.copy(w_turned[:, :], w_ps[:, :]).then_inc(w_ready, 1)

            def carry_turned(pair, half, group):
                act.wait_ge(group_turned, pair * 2 * GROUPS + (half * GROUPS + group + 1))
                act.copy(x_turned[group % 2][:, :, :], turned_ps[group % 2][:, 0:GROUP, :]).then_inc(x_turned_ready, 1)

            def load_ahead(pair, half, load):
                a, b = load_range(load)
                act.dma_start(x_in[half][:, a:b, :],
                              x[bass.ds(pair * 2 * P + (half + 2) * P, P), a:b, :]).then_inc(x_loaded[half][load], 16)

            def carry_projected(pair, half, group):
                a, b = group_range(group)
                act.wait_ge(group_projected, pair * 2 * GROUPS + (half * GROUPS + group + 1))
                act.copy(proj[:, half, a:b, :], proj_ps[group % 2][:, 0:GROUP, :]).then_inc(proj_ready, 1)

            def carry_tile(pair, half, loads):
                act.wait_ge(proj_free, pair * 2 + (half + 1))
                carry_turned(pair, half, 0)
                for group in range(1, GROUPS):
                    carry_turned(pair, half, group)
                    if loads and group % GROUPS_PER_LOAD == GROUPS_PER_LOAD - 1:
                        load_ahead(pair, half, group // GROUPS_PER_LOAD)
                    carry_projected(pair, half, group - 1)
                carry_projected(pair, half, GROUPS - 1)

            with act.Fori(0, tiles // 2 - 1) as pair:
                for half in range(2):
                    carry_tile(pair, half, loads=True)
            for half in range(2):
                carry_tile(tiles // 2 - 1, half, loads=False)

        @block.vector
        def _(dve):
            def multiply_chunk(tile, chunk):
                slot = chunk % SLOTS
                first_group = groups_for(chunk - 1)
                for i, j, count, place in chunk_rows(chunk):
                    group = group_of(i)
                    if group >= first_group:
                        first_group = group + 1
                        dve.wait_ge(proj_ready, tile * GROUPS + (group + 1))
                    last = dve.tensor_tensor(
                        products[slot][:, place:place + count, :],
                        proj[:, tile % 2, i:i + 1, :].broadcast_to([P, count, DIM]),
                        proj[:, tile % 2, j:j + count, :], ALU.mult)
                last.then_inc(chunk_ready, 1)

            def give_back(tile):
                dve.wait_ge(chunk_ready, tile * CHUNKS + CHUNKS)
                dve.sem_inc(proj_free, 1)

            dve.sem_inc(proj_free, 2)
            for chunk in range(CHUNKS):
                if chunk >= SLOTS:
                    dve.wait_ge(stored[chunk % SLOTS], 16 * (chunk // SLOTS))
                multiply_chunk(0, chunk)
            give_back(0)
            with dve.Fori(1, tiles) as tile:
                for chunk in range(CHUNKS):
                    dve.wait_ge(stored[chunk % SLOTS], 16 * ROUNDS * tile + 16 * (chunk // SLOTS))
                    multiply_chunk(tile, chunk)
                give_back(tile)


_INS = ["r_x", "L0_rec_W"]


def kernel(**inputs):
    import concourse.bacc as _bacc
    from concourse.bass_utils import run_bass_kernel_spmd as _run

    nc = _bacc.Bacc("TRN2", target_bir_lowering=False, num_devices=1)
    arrays, args = {}, []
    for name in _INS:
        a = np.ascontiguousarray(inputs[name])
        arrays[f"in_{name}_dram"] = a
        args.append(nc.dram_tensor(f"in_{name}_dram", a.shape, mybir.dt.from_np(a.dtype), kind="ExternalInput").ap())
    shape = (inputs["r_x"].shape[0], PAIRS, DIM)
    args.append(nc.dram_tensor("out_dram", shape, mybir.dt.float32, kind="ExternalOutput").ap())
    pairwise_products(nc, *args)
    r = _run(nc, [arrays], core_ids=[0])
    return r.results[0]["out_dram"]
```
